# Optimizing a Trainium2 kernel written in Bass

```python
import numpy as np
import jax
import jax.numpy as jnp

def _softmax(x, axis=-1):
    return jax.nn.softmax(x, axis=axis)

def _gelu(x):
    return jax.nn.gelu(x, approximate=True)

def _silu(x):
    return jax.nn.silu(x)

def _sigmoid(x):
    return jax.nn.sigmoid(x)

def _layernorm(x, axis=-1, eps=1e-05):
    m = jnp.mean(x, axis=axis, keepdims=True)
    v = jnp.var(x, axis=axis, keepdims=True)
    return (x - m) / jnp.sqrt(v + eps)

def _scatter_add(tgt, idx, src, axis=0):
    return tgt.at[idx].add(src)

def _segment_sum(src, seg, n):
    return jax.ops.segment_sum(src, seg, n)
kernel_name = 'mk_adj_resnorm_d2_adj_r2_ef6337'

def setup_inputs(seed: int=0):
    np.random.seed(seed)
    _w = jnp.asarray

    def _rec_inputs():
        import jax
        import jax.numpy as jnp
        _gk = jax.random.key(seed)
        x = -0.0005207 + 1.001 * jax.random.normal(jax.random.fold_in(_gk, 1), (8192, 128), jnp.float32)
        _a = jax.random.bernoulli(jax.random.fold_in(_gk, 2), 0.00195312, (8192, 8192))
        _a = jnp.logical_or(_a, jnp.swapaxes(_a, -1, -2))
        _a = jnp.logical_or(_a, jnp.eye(8192, dtype=bool))
        _af = _a.astype(jnp.float32)
        _af = _af * jax.random.uniform(jax.random.fold_in(_gk, 3), (8192, 8192), jnp.float32, 0.05, 1)
        adj = _af
        return (x, adj)
    x, adj = _rec_inputs()

    def _L0_gnn_setup():
        import jax, jax.numpy as jnp
        import numpy as np
        ALPHA = 0.1
        N, F = (8192, 128)
        key = jax.random.key(seed)
        k1, k2, k3 = jax.random.split(key, 3)
        x = jax.random.normal(k1, (N, F), dtype=jnp.float32)
        adj = jax.random.uniform(k2, (N, N), dtype=jnp.float32)
        h = jax.random.normal(k3, (N, F), dtype=jnp.float32)
        return {'x': x, 'adj': adj, 'h': h}
    _L0_gnn_all = _L0_gnn_setup()
    _L0_gnn_in = {k: v for k, v in _L0_gnn_all.items() if k in ('h',)}
    del _L0_gnn_all

    def _L1_gnn_setup():
        import jax, jax.numpy as jnp
        import numpy as np
        OVERFLOW_MARGIN = 1e-08
        N, D, OUT = (4096, 128, 128)
        key = jax.random.key(seed)
        k1, k2, k3 = jax.random.split(key, 3)
        values = jax.random.normal(k1, (N, D), dtype=jnp.float32)
        adjacency = jax.random.uniform(k2, (N, N), dtype=jnp.float32)
        W = jax.random.normal(k3, (D, OUT), dtype=jnp.float32) * 0.05
        b = jnp.zeros((OUT,), dtype=jnp.float32)
        return {'values': values, 'adjacency': adjacency, 'W': W, 'b': b}
    _L1_gnn_all = _L1_gnn_setup()
    _L1_gnn_in = {k: v for k, v in _L1_gnn_all.items() if k in ('W', 'b')}
    del _L1_gnn_all
    return {'x': x, 'adj': adj, 'L0_gnn_h': _L0_gnn_in['h'], 'L1_gnn_W': _L1_gnn_in['W'], 'L1_gnn_b': _L1_gnn_in['b']}

def reference(x, adj, L0_gnn_h, L1_gnn_W, L1_gnn_b):
    import jax
    import jax.numpy as jnp

    def _L0_gnn_ref(x, adj, h):
        import jax, jax.numpy as jnp
        import numpy as np
        ALPHA = 0.1
        N, F = (8192, 128)
        return (1.0 - ALPHA) * (adj @ x) + ALPHA * h

    def _L1_gnn_ref(values, adjacency, W, b):
        import jax, jax.numpy as jnp
        import numpy as np
        OVERFLOW_MARGIN = 1e-08
        N, D, OUT = (4096, 128, 128)
        fc_sc = values @ W + b
        d = jnp.sum(adjacency, axis=1)
        d_inv_sqrt = 1.0 / (jnp.sqrt(d) + OVERFLOW_MARGIN)
        laplacian = adjacency * d_inv_sqrt[:, None] * d_inv_sqrt[None, :]
        return laplacian @ fc_sc
    x = _layernorm(x + _L0_gnn_ref(x, adj, L0_gnn_h), axis=-1)
    x = _layernorm(x + _L1_gnn_ref(x, adj, L1_gnn_W, L1_gnn_b), axis=-1)
    return x

_drawn_inputs = setup_inputs


def setup_inputs(seed=0):
    import zlib

    import numpy as np

    out = dict(_drawn_inputs(seed))
    spreads = {'L1_gnn_b': (0.0, 0.1)}
    factors = {}
    for name, (base, spread) in spreads.items():
        noise = np.random.default_rng([zlib.crc32(name.encode()), seed]).standard_normal(out[name].shape)
        drawn = base * np.exp(spread * noise) if base else spread * noise
        out[name] = jnp.asarray(drawn.astype(out[name].dtype))
    for name, factor in factors.items():
        out[name] = (out[name] * factor).astype(out[name].dtype)
    return out
```

```python
from contextlib import ExitStack

import concourse.bass as bass
from concourse import mybir

F32 = mybir.dt.float32
F32R = mybir.dt.float32r
ACT = mybir.ActivationFunctionType
ALU = mybir.AluOpType
AX_X = mybir.AxisListType.X

P = 128
QUAD = 32
QUADS = P // QUAD
ROWS = 512
GROUPS = ROWS // QUAD
TILES = ROWS // P
CHUNK_SLICES = 8
RING = 4
BATCH = 4
SPLITS = BATCH - 1
TURNED = 4
PARTS = 2
LN_EPS = 1e-5
OVERFLOW_MARGIN = 1e-8
ALPHA = 0.1


def bass_adj_resnorm(nc, x, adj, h, w, b, out):
    N, F = x.shape
    assert F == P and N % (QUADS * QUAD * CHUNK_SLICES) == 0
    QCOLS = N // QUADS
    SLICES = QCOLS // QUAD
    CHUNKS = SLICES // CHUNK_SLICES
    CCOLS = CHUNK_SLICES * QUAD
    BATCHES = SLICES // BATCH
    PER_CHUNK = CHUNK_SLICES // BATCH
    BLOCKS = N // ROWS
    PAIRS = BLOCKS // 2
    PIECE = CHUNK_SLICES
    PIECES = CHUNKS
    assert CHUNKS % RING == 0 and BATCHES % TURNED == 0 and BLOCKS % 2 == 0 and PER_CHUNK == 2
    FULLS = SLICES // BATCH
    SLOT_USES = CHUNKS // RING
    LOAD = 16 * QUADS

    def by_vector(k):
        return k % 2 == 0

    adj_v = adj.rearrange("(k g r) c -> k r g c", g=GROUPS, r=QUAD)
    x_v = x.rearrange("(k t p) f -> k p t f", t=TILES, p=P)
    h_v = h.rearrange("(k t p) f -> k p t f", t=TILES, p=P)
    out_v = out.rearrange("(k t p) f -> k p t f", t=TILES, p=P)
    x1_d = nc.dram_tensor("x1_scratch", (N, F), F32).ap()
    y_d = nc.dram_tensor("y_scratch", (N, F), F32).ap()
    yparts_d = nc.dram_tensor("yparts_scratch", (N, 2, F), F32).ap()
    x1_v = x1_d.rearrange("(k t p) f -> k p t f", t=TILES, p=P)
    y_v = y_d.rearrange("(k t p) f -> k p t f", t=TILES, p=P)
    yparts_v = yparts_d.rearrange("(k t p) s f -> k p t (s f)", t=TILES, p=P)

    with ExitStack() as ctx:
        def sb(name, shape, dt=F32):
            return ctx.enter_context(nc.sbuf_tensor(name, shape, dt))

        def psum(name, shape):
            return ctx.enter_context(nc.psum_tensor(name, shape, F32))

        def sem(name):
            return ctx.enter_context(nc.semaphore(name))

        adj_in = sb("adj_in", [P, RING, GROUPS, CCOLS])
        turned = [sb(f"turned{t}", [P, SPLITS if by_vector(t) else BATCH, ROWS]) for t in range(TURNED)]
        high = sb("high", [P, PARTS, SPLITS, ROWS], F32R)
        low = sb("low", [P, PARTS, SPLITS, ROWS], F32R)
        op_full = sb("op_full", [P, FULLS, F])
        op_split = sb("op_split", [P, FULLS * SPLITS, 2, F], F32R)
        x_stage = sb("x_stage", [P, 2, PIECE, F])
        x_sum = sb("x_sum", [P, 2, PIECE])
        acc_sb = sb("acc_sb", [P, ROWS])
        resid = sb("resid", [P, TILES, F])
        h_nat = sb("h_nat", [P, TILES, F])
        xh = sb("xh", [P, TILES, F])
        pre = sb("pre", [P, TILES, F])
        normed = sb("normed", [P, TILES, F])
        x1T = sb("x1T", [P, ROWS])
        fc = sb("fc", [P, TILES, F])
        y = sb("y", [P, TILES, F])
        y_parts = sb("y_parts", [P, TILES, 2, F], F32R)
        junk = sb("junk", [P, TILES, F])
        w_sb = sb("w_sb", [P, F])
        b_sb = sb("b_sb", [P, F])
        ident = sb("ident", [P, P])
        eps_sb = sb("eps_sb", [P, 1])
        last_col = sb("last_col", [P, TILES])
        deg_root = sb("deg_root", [P, TILES])
        dinv = sb("dinv", [P, TILES])
        dinv_all = sb("dinv_all", [P, BLOCKS * TILES])
        bn = sb("bn", [P, TILES, 6])
        fence = sb("fence", [P, 1])
        meanvar = sb("meanvar", [P, TILES, 2])
        std = sb("std", [P, TILES])
        rstd = sb("rstd", [P, TILES])
        shift = sb("shift", [P, TILES])

        acc = [psum(f"acc{i}", [P, ROWS]) for i in range(2)]
        turned_ps = [psum(f"turned_ps{i}", [P, ROWS]) for i in range(2)]
        nat = psum("nat", [P, TILES, F])
        x1T_ps = psum("x1T_ps", [P, ROWS])
        fc_ps = psum("fc_ps", [P, TILES, F])

        adj_loaded = [sem(f"adj_loaded{s}") for s in range(RING)]
        x_loaded = [sem(f"x_loaded{s}") for s in range(2)]
        const_loaded = sem("const_loaded")
        ident_zero = sem("ident_zero")
        ident_ready = sem("ident_ready")
        eps_ready = sem("eps_ready")
        x_summed = sem("x_summed")
        x_shift_ready = sem("x_shift_ready")
        x_shifted = sem("x_shifted")
        x_centred = sem("x_centred")
        x_high = sem("x_high")
        x_full = sem("x_full")
        x_low = sem("x_low")
        turned_ready = sem("turned_ready")
        turned_ps_ready = sem("turned_ps_ready")
        high_ready = sem("high_ready")
        high_ps_ready = sem("high_ps_ready")
        low_ready = sem("low_ready")
        low_ps_ready = sem("low_ps_ready")
        multiplied = sem("multiplied")
        acc_copied = sem("acc_copied")
        nat_ready = sem("nat_ready")
        resid_loaded = sem("resid_loaded")
        h_loaded = sem("h_loaded")
        last_col_ready = sem("last_col_ready")
        xh_ready = sem("xh_ready")
        dinv_cur = sem("dinv_cur")
        scaled = sem("scaled")
        pre_ready = sem("pre_ready")
        deg_shift = sem("deg_shift")
        dinv_ready = sem("dinv_ready")
        dinv_kept = sem("dinv_kept")
        bn_ready = sem("bn_ready")
        stats_ready = sem("stats_ready")
        std_ready = sem("std_ready")
        rstd_ready = sem("rstd_ready")
        shift_ready = sem("shift_ready")
        normed_ready = sem("normed_ready")
        normed_stored = sem("normed_stored")
        x1T_ready = sem("x1T_ready")
        x1T_copied = sem("x1T_copied")
        fc_done = sem("fc_done")
        fc_ready = sem("fc_ready")
        y_ready = sem("y_ready")
        y_high_ready = sem("y_high_ready")
        y_low_ready = sem("y_low_ready")
        y_stored = sem("y_stored")
        yparts_stored = sem("yparts_stored")
        y_loaded = [sem(f"y_loaded{c}") for c in range(CHUNKS)]

        def walk(eng, pair):
            pair(0, 1, None)
            with eng.Fori(1, PAIRS) as i:
                pair(i, 1, 1)
            pair(PAIRS, 2, 1)
            with eng.Fori(PAIRS + 1, 2 * PAIRS - 1) as i:
                pair(i, 2, 2)
            pair(2 * PAIRS - 1, 2, 2)

        def load_adj(eng, quads, block, c):
            for a in quads:
                cols = slice(a * QCOLS + c * CCOLS, a * QCOLS + (c + 1) * CCOLS)
                eng.dma_start(adj_in[a * QUAD:(a + 1) * QUAD, c % RING, :, :],
                              adj_v[block, :, :, cols]).then_inc(adj_loaded[c % RING], 16)

        block = ctx.enter_context(nc.Block())

        @block.sync
        def _(sp):
            def load_x(q):
                if q >= 2:
                    sp.wait_ge(x_low, q - 1)
                    sp.wait_ge(x_full, q - 1)
                for a in range(QUADS):
                    rows = slice(a * QCOLS + q * PIECE * QUAD, a * QCOLS + (q + 1) * PIECE * QUAD)
                    sp.dma_start(x_stage[a * QUAD:(a + 1) * QUAD, q % 2, :, :],
                                 x[rows, :].rearrange("(s c) f -> c s f", c=QUAD)).then_inc(x_loaded[q % 2], 16)

            def load_y(c):
                sp.wait_ge(multiplied, (BLOCKS - 1) * BATCHES + PER_CHUNK * (c + 1))
                stored = BLOCKS - BLOCKS // QUADS + (c * CCOLS) // ROWS + 1
                sp.wait_ge(y_stored, 16 * stored)
                sp.wait_ge(yparts_stored, 16 * stored)
                for a in range(QUADS):
                    part = slice(a * QUAD, (a + 1) * QUAD)
                    rows = slice(a * QCOLS + c * CCOLS, a * QCOLS + (c + 1) * CCOLS)
                    yq = y_d[rows, :].rearrange("(k s c) f -> s c k f", s=BATCH, c=QUAD)
                    sp.dma_start(op_full[part, c * PER_CHUNK:(c + 1) * PER_CHUNK, :],
                                 yq[0]).then_inc(y_loaded[c], 16)
                    ypq = yparts_d[rows, :, :].rearrange("(k s c) h f -> k c s (h f)", s=BATCH, c=QUAD)
                    for k in range(PER_CHUNK):
                        s0 = (c * PER_CHUNK + k) * SPLITS
                        sp.dma_start(op_split[part, s0:s0 + SPLITS, :, :].bitcast(F32).rearrange("p s h f -> p s (h f)"),
                                     ypq[k, :, 1:BATCH, :]).then_inc(y_loaded[c], 16)

            def pair(i, layer, before):
                for par in range(2):
                    g = 2 * i + par
                    blk = g if layer == 1 else g - BLOCKS
                    peeled = before != layer and par == 0
                    for c in range(CHUNKS):
                        if not (peeled and layer == 1 and c < RING):
                            sp.wait_ge(turned_ready, g * BATCHES + PER_CHUNK * (c - RING + 1))
                            if peeled and layer == 1:
                                load_x(c)
                        load_adj(sp, (0, 1), blk, c)
                        if peeled and layer == 1 and c == RING - 1:
                            load_x(2)
                            load_x(3)
                        if peeled and layer == 1 and c == 0:
                            sp.dma_start(w_sb[:, :], w).then_inc(const_loaded, 16)
                            sp.dma_start(b_sb[:, :], b.rearrange("(a n) -> a n", a=1).to_broadcast((P, F))
                                         ).then_inc(const_loaded, 16)
                        if peeled and layer == 2:
                            load_y(c)
                        if c == CHUNKS - 2:
                            if not (peeled and layer == 1):
                                sp.wait_ge(pre_ready, g)
                            if layer == 1:
                                sp.dma_start(resid[:, :, :], x_v[blk]).then_inc(resid_loaded, 16)
                                sp.dma_start(h_nat[:, :, :], h_v[blk]).then_inc(h_loaded, 16)
                            else:
                                sp.wait_ge(normed_stored, 16 * (blk + 1))
                                sp.dma_start(resid[:, :, :], x1_v[blk]).then_inc(resid_loaded, 16)

            load_x(0)
            load_x(1)
            walk(sp, pair)
            sp.wait_ge(normed_stored, 16 * 2 * BLOCKS)

        @block.vector
        def _(dve):
            def centre(q):
                s = q % 2
                dve.wait_ge(x_loaded[s], 16 * QUADS * (q // 2 + 1))
                nc.vector.tensor_reduce(x_sum[:, s, :], x_stage[:, s, :, :], AX_X, ALU.add).then_inc(x_summed, 1)
                dve.wait_ge(x_summed, q + 1)
                nc.vector.tensor_scalar(x_sum[:, s, :], x_sum[:, s, :], -1.0 / F, None,
                                        ALU.mult).then_inc(x_shift_ready, 1)
                dve.wait_ge(x_shift_ready, q + 1)
                nc.vector.tensor_tensor(x_stage[:, s, :, :], x_stage[:, s, :, :],
                                        x_sum[:, s, :].unsqueeze(2).to_broadcast((P, PIECE, F)),
                                        ALU.add).then_inc(x_shifted, 1)
                dve.wait_ge(x_shifted, q + 1)
                nc.vector.memset(x_stage[:, s, :, F - 1], 1.0).then_inc(x_centred, 1)

            def finish(k, g, layer):
                if k == 5 and layer == 1:
                    dve.wait_ge(resid_loaded, 16 * (g + 1))
                    dve.wait_ge(h_loaded, 16 * (g + 1))
                    nc.vector.scalar_tensor_tensor(xh[:, :, :], h_nat[:, :, :], ALPHA, resid[:, :, :],
                                                   ALU.mult, ALU.add).then_inc(xh_ready, 1)
                    dve.wait_ge(xh_ready, g + 1)
                    dve.wait_ge(last_col_ready, g + 1)
                    nc.vector.scalar_tensor_tensor(pre[:, :, 0:F - 1], nat[:, :, 0:F - 1], 1.0 - ALPHA,
                                                   xh[:, :, 0:F - 1], ALU.mult, ALU.add)
                    nc.vector.scalar_tensor_tensor(pre[:, :, F - 1], last_col[:, :], 1.0 - ALPHA,
                                                   xh[:, :, F - 1], ALU.mult, ALU.add).then_inc(pre_ready, 1)
                    nc.vector.tensor_scalar(deg_root[:, :], deg_root[:, :], OVERFLOW_MARGIN, None,
                                            ALU.add).then_inc(deg_shift, 1)
                    dve.wait_ge(deg_shift, g + 1)
                    nc.vector.reciprocal(dinv[:, :], deg_root[:, :]).then_inc(dinv_ready, 1)
                    dve.wait_ge(dinv_ready, g + 1)
                    nc.vector.tensor_copy(dinv_all[:, bass.ts(g, TILES)], dinv[:, :]).then_inc(dinv_kept, 1)
                if k == 5 and layer == 2:
                    dve.wait_ge(resid_loaded, 16 * (g + 1))
                    dve.wait_ge(scaled, g - BLOCKS + 1)
                    nc.vector.tensor_tensor(pre[:, :, :], xh[:, :, :], resid[:, :, :],
                                            ALU.add).then_inc(pre_ready, 1)
                if k == 5:
                    dve.wait_ge(pre_ready, g + 1)
                    for t in range(TILES):
                        last = nc.vector.bn_stats(bn[:, t, :], pre[:, t, :])
                    last.then_inc(bn_ready, 1)
                    dve.wait_ge(bn_ready, g + 1)
                    nc.vector.tensor_copy(fence[:, :], bn[:, 0, 0:1])
                    for t in range(TILES):
                        last = nc.vector.bn_aggr(meanvar[:, t, :], bn[:, t, :])
                    last.then_inc(stats_ready, 1)
                if k == 7:
                    dve.wait_ge(std_ready, g + 1)
                    nc.vector.reciprocal(rstd[:, :], std[:, :]).then_inc(rstd_ready, 1)
                    dve.wait_ge(rstd_ready, g + 1)
                    nc.vector.scalar_tensor_tensor(shift[:, :], meanvar[:, :, 0], -1.0, rstd[:, :],
                                                   ALU.mult, ALU.mult).then_inc(shift_ready, 1)
                if k == 10 and layer == 1:
                    dve.wait_ge(fc_done, g + 1)
                    nc.vector.tensor_tensor(fc[:, :, :], fc_ps[:, :, :],
                                            b_sb[:, :].unsqueeze(1).to_broadcast((P, TILES, F)),
                                            ALU.add).then_inc(fc_ready, 1)
                if k == 12 and layer == 1:
                    dve.wait_ge(y_high_ready, g + 1)
                    nc.vector.tensor_tensor(y_parts[:, :, 1, :], y[:, :, :], y_parts[:, :, 0, :].bitcast(F32),
                                            ALU.subtract).then_inc(y_low_ready, 1)

            def low_of_psum(n, k, even):
                dve.wait_ge(high_ps_ready, even + 1)
                nc.vector.tensor_tensor(low[:, k % PARTS, SPLITS - 1, :], turned_ps[k // 2 % 2][:, :],
                                        high[:, k % PARTS, SPLITS - 1, :].bitcast(F32),
                                        ALU.subtract).then_inc(low_ps_ready, 1)

            def pair(i, layer, before):
                for par in range(2):
                    g = 2 * i + par
                    first = before is None and par == 0
                    for k in range(BATCHES):
                        n = g * BATCHES + k
                        even = g * (BATCHES // 2) + k // 2
                        c = k // PER_CHUNK
                        if k % PER_CHUNK == 0:
                            use = g * SLOT_USES + c // RING + 1
                            dve.wait_ge(adj_loaded[c % RING], use * LOAD)
                        if not (first and k < TURNED):
                            dve.wait_ge(multiplied, n - TURNED + 1)
                        s0 = k % PER_CHUNK * BATCH
                        m = BATCH - 1 if by_vector(k) else BATCH
                        view = adj_in[:, c % RING, :, :].rearrange("p g (s c) -> p s g c", c=QUAD)
                        nc.vector.transpose(
                            turned[k % TURNED][:, :, :].rearrange("p s (g r) -> p s g r", r=QUAD),
                            view[:, s0:s0 + m, :, :]).then_inc(turned_ready, 1)
                        if by_vector(k):
                            nc.vector.transpose(turned_ps[k // 2 % 2][:, :].rearrange("p (g r) -> p g r", r=QUAD),
                                                view[:, s0 + m, :, :]).then_inc(turned_ps_ready, 1)
                        else:
                            low_of_psum(n - 1, k - 1, even)
                        if first and k % 2 == 1 and 2 + k // 2 < PIECES:
                            centre(2 + k // 2)
                        if par == 1:
                            finish(k, g - 1, layer)
                        elif before is not None:
                            finish(k, g - 1, before)

            nc.vector.memset(eps_sb[:, :], LN_EPS).then_inc(eps_ready, 1)
            centre(0)
            centre(1)
            walk(dve, pair)
            for k in range(BATCHES):
                finish(k, 2 * BLOCKS - 1, 2)

        @block.scalar
        def _(act):
            def prepare(q):
                s = q % 2
                act.wait_ge(x_centred, q + 1)
                view = x_stage[:, s, :, :].rearrange("p (k s) f -> p k s f", s=BATCH)
                nc.scalar.copy(op_full[:, q * PER_CHUNK:(q + 1) * PER_CHUNK, :], view[:, :, 0, :]).then_inc(x_full, 1)
                splits = slice(q * PER_CHUNK * SPLITS, (q + 1) * PER_CHUNK * SPLITS)
                nc.scalar.copy(op_split[:, splits, 0, :].rearrange("p (k s) f -> p k s f", s=SPLITS),
                               view[:, :, 1:BATCH, :]).then_inc(x_high, 1)

            def finish(k, g, layer, par):
                if k == 1:
                    act.wait_ge(multiplied, (g + 1) * BATCHES)
                    nc.scalar.copy(acc_sb[:, :], acc[par][:, :]).then_inc(acc_copied, 1)
                if k == 3:
                    act.wait_ge(nat_ready, g + 1)
                if k == 3 and layer == 1:
                    for t in range(TILES):
                        nc.scalar.activation(junk[:, t, 0:F - 1], nat[:, t, 0:F - 1], ACT.Copy, scale=-1.0,
                                             accum_out=last_col[:, t:t + 1])
                    nc.scalar.activation(deg_root[:, :], nat[:, :, F - 1], ACT.Sqrt).then_inc(last_col_ready, 1)
                if k == 3 and layer == 2:
                    nc.scalar.copy(dinv[:, :], dinv_all[:, bass.ts(g - BLOCKS, TILES)]).then_inc(dinv_cur, 1)
                    act.wait_ge(dinv_cur, g - BLOCKS + 1)
                    for t in range(TILES):
                        last = nc.scalar.activation(xh[:, t, :], nat[:, t, :], ACT.Copy, scale=dinv[:, t:t + 1])
                    last.then_inc(scaled, 1)
                if k == 5:
                    act.wait_ge(stats_ready, g + 1)
                    nc.scalar.activation(std[:, :], meanvar[:, :, 1], ACT.Sqrt,
                                         bias=eps_sb[:, 0:1]).then_inc(std_ready, 1)
                if k == 6:
                    act.wait_ge(shift_ready, g + 1)
                    if not (isinstance(g, int) and g == 0):
                        act.wait_ge(normed_stored, 16 * g)
                    for t in range(TILES):
                        last = nc.scalar.activation(normed[:, t, :], pre[:, t, :], ACT.Identity,
                                                    bias=shift[:, t:t + 1], scale=rstd[:, t:t + 1])
                    last.then_inc(normed_ready, 1)
                    act.wait_ge(normed_ready, g + 1)
                    rows = x1_v[g] if layer == 1 else out_v[g - BLOCKS]
                    act.dma_start(rows, normed[:, :, :]).then_inc(normed_stored, 16)
                if k == 8 and layer == 1:
                    act.wait_ge(x1T_ready, g + 1)
                    nc.scalar.copy(x1T[:, :], x1T_ps[:, :]).then_inc(x1T_copied, 1)
                if k == 10 and layer == 1:
                    act.wait_ge(fc_ready, g + 1)
                    if not (isinstance(g, int) and g == 0):
                        act.wait_ge(y_stored, 16 * g)
                        act.wait_ge(yparts_stored, 16 * g)
                    for t in range(TILES):
                        last = nc.scalar.activation(y[:, t, :], fc[:, t, :], ACT.Copy, scale=dinv[:, t:t + 1])
                    last.then_inc(y_ready, 1)
                    act.wait_ge(y_ready, g + 1)
                    nc.scalar.copy(y_parts[:, :, 0, :], y[:, :, :]).then_inc(y_high_ready, 1)
                    act.dma_start(y_v[g], y[:, :, :]).then_inc(y_stored, 16)
                if k == 11 and layer == 1:
                    act.wait_ge(y_low_ready, g + 1)
                    act.wait_ge(y_high_ready, g + 1)
                    act.dma_start(yparts_v[g], y_parts[:, :, :, :].bitcast(F32).rearrange("p t h f -> p t (h f)")
                                  ).then_inc(yparts_stored, 16)

            def pair(i, layer, before):
                for par in range(2):
                    g = 2 * i + par
                    blk = g if layer == 1 else g - BLOCKS
                    first = before is None and par == 0
                    for k in range(BATCHES):
                        n = g * BATCHES + k
                        even = g * (BATCHES // 2) + k // 2
                        parts = slice(0, SPLITS - 1 if by_vector(k) else SPLITS)
                        if not (first and k < PARTS):
                            act.wait_ge(multiplied, n - PARTS + 1)
                        act.wait_ge(turned_ready, n + 1)
                        nc.scalar.copy(high[:, k % PARTS, parts, :],
                                       turned[k % TURNED][:, 1:, :]).then_inc(high_ready, 1)
                        if by_vector(k):
                            act.wait_ge(turned_ps_ready, even + 1)
                            nc.scalar.copy(high[:, k % PARTS, SPLITS - 1, :],
                                           turned_ps[k // 2 % 2][:, :]).then_inc(high_ps_ready, 1)
                        if first and k % 2 == 1 and 2 + k // 2 < PIECES:
                            prepare(2 + k // 2)
                        if k % PER_CHUNK == PER_CHUNK - 1:
                            c = k // PER_CHUNK + RING
                            if c < CHUNKS:
                                load_adj(act, (2, 3), blk, c)
                            elif not (isinstance(i, int) and i == 2 * PAIRS - 1 and par == 1):
                                load_adj(act, (2, 3), (g + 1) % BLOCKS, c - CHUNKS)
                        if par == 1:
                            finish(k, g - 1, layer, 0)
                        elif before is not None:
                            finish(k, g - 1, before, 1)

            for c in range(RING):
                load_adj(act, (2, 3), 0, c)
            act.wait_ge(eps_ready, 1)
            prepare(0)
            prepare(1)
            walk(act, pair)
            for k in range(BATCHES):
                finish(k, 2 * BLOCKS - 1, 2, 1)

        @block.gpsimd
        def _(pool):
            def prepare(q):
                s = q % 2
                pool.wait_ge(x_high, q + 1)
                splits = slice(q * PER_CHUNK * SPLITS, (q + 1) * PER_CHUNK * SPLITS)
                view = op_split[:, splits, :, :].rearrange("p (k s) h f -> p k s h f", s=SPLITS)
                for k in range(PER_CHUNK):
                    last = nc.gpsimd.tensor_tensor(view[:, k, :, 1, :],
                                                   x_stage[:, s, k * BATCH + 1:(k + 1) * BATCH, :],
                                                   view[:, k, :, 0, :].bitcast(F32), ALU.subtract)
                last.then_inc(x_low, 1)

            def pair(i, layer, before):
                for par in range(2):
                    g = 2 * i + par
                    first = before is None and par == 0
                    for k in range(BATCHES):
                        n = g * BATCHES + k
                        parts = slice(0, SPLITS - 1 if by_vector(k) else SPLITS)
                        pool.wait_ge(high_ready, n + 1)
                        nc.gpsimd.tensor_tensor(low[:, k % PARTS, parts, :], turned[k % TURNED][:, 1:, :],
                                                high[:, k % PARTS, parts, :].bitcast(F32),
                                                ALU.subtract).then_inc(low_ready, 1)
                        if first and k % 2 == 1 and 2 + k // 2 < PIECES:
                            prepare(2 + k // 2)

            nc.gpsimd.memset(ident[:, :], 0.0).then_inc(ident_zero, 1)
            pool.wait_ge(ident_zero, 1)
            nc.gpsimd.affine_select(out=ident[:, :], in_=ident[:, :], compare_op=ALU.not_equal, fill=1.0, base=0,
                                    pattern=[[-1, P]], channel_multiplier=1).then_inc(ident_ready, 1)
            prepare(0)
            prepare(1)
            walk(pool, pair)

        @block.tensor
        def _(pe):
            def finish(k, g, layer):
                if k == 1:
                    pe.wait_ge(acc_copied, g + 1)
                    for t in range(TILES):
                        last = nc.tensor.transpose(nat[:, t, :], acc_sb[:, t * P:(t + 1) * P], ident[:, :])
                    last.then_inc(nat_ready, 1)
                if k == 5 and layer == 1:
                    pe.wait_ge(normed_ready, g + 1)
                    for t in range(TILES):
                        last = nc.tensor.transpose(x1T_ps[:, t * P:(t + 1) * P], normed[:, t, :], ident[:, :])
                    last.then_inc(x1T_ready, 1)
                if k == 7 and layer == 1:
                    pe.wait_ge(x1T_copied, g + 1)
                    for t in range(TILES):
                        last = nc.tensor.matmul(fc_ps[:, t, :], x1T[:, t * P:(t + 1) * P], w_sb[:, :],
                                                start=True, stop=True)
                    last.then_inc(fc_done, 1)

            def pair(i, layer, before):
                for par in range(2):
                    g = 2 * i + par
                    first = before is None and par == 0
                    for k in range(BATCHES):
                        n = g * BATCHES + k
                        even = g * (BATCHES // 2) + k // 2
                        if first and k % PER_CHUNK == 0:
                            pe.wait_ge(x_full, k // PER_CHUNK + 1)
                            pe.wait_ge(x_low, k // PER_CHUNK + 1)
                        if before is not None and before != layer and par == 0 and k % PER_CHUNK == 0:
                            pe.wait_ge(y_loaded[k // PER_CHUNK], 16 * QUADS * (1 + PER_CHUNK))
                        to = acc[par][:, :]
                        ops = [op_split[:, k * SPLITS + s, :, :] for s in range(SPLITS)]
                        highs = [high[:, k % PARTS, s, :] for s in range(SPLITS)]
                        pe.wait_ge(turned_ready, n + 1)
                        nc.tensor.matmul(to, op_full[:, k, :], turned[k % TURNED][:, 0, :],
                                         start=k == 0, stop=False)
                        pe.wait_ge(high_ready, n + 1)
                        for s in range(SPLITS):
                            if s == SPLITS - 1 and by_vector(k):
                                pe.wait_ge(high_ps_ready, even + 1)
                            nc.tensor.matmul(to, ops[s][:, 1, :], highs[s], start=False, stop=False)
                            nc.tensor.matmul(to, ops[s][:, 0, :], highs[s], start=False, stop=False)
                        pe.wait_ge(low_ready, n + 1)
                        for s in range(SPLITS):
                            if s == SPLITS - 1 and by_vector(k):
                                pe.wait_ge(low_ps_ready, even + 1)
                            last = nc.tensor.matmul(to, ops[s][:, 0, :], low[:, k % PARTS, s, :], start=False,
                                                    stop=k == BATCHES - 1 and s == SPLITS - 1)
                        last.then_inc(multiplied, 1)
                        if par == 1:
                            finish(k, g - 1, layer)
                        elif before is not None:
                            finish(k, g - 1, before)

            pe.wait_ge(ident_ready, 1)
            pe.wait_ge(const_loaded, 32)
            walk(pe, pair)
            for k in range(BATCHES):
                finish(k, 2 * BLOCKS - 1, 2)


_INS = ['x', 'adj', 'L0_gnn_h', 'L1_gnn_W', 'L1_gnn_b']


def kernel(**inputs):
    import numpy as _np
    import concourse.bacc as _bacc
    from concourse import mybir as _mybir
    from concourse.bass_utils import run_bass_kernel_spmd as _run

    nc = _bacc.Bacc("TRN2", target_bir_lowering=False, num_devices=1)
    arrays, args = {}, []
    for name in _INS:
        a = _np.ascontiguousarray(inputs[name])
        arrays[f"in_{name}_dram"] = a
        args.append(nc.dram_tensor(f"in_{name}_dram", a.shape, _mybir.dt.from_np(a.dtype), kind="ExternalInput").ap())
    out = nc.dram_tensor("out_0_dram", inputs["x"].shape, _mybir.dt.float32, kind="ExternalOutput").ap()
    bass_adj_resnorm(nc, *args, out)
    r = _run(nc, [arrays], core_ids=[0])
    return r.results[0]["out_0_dram"]
```

```python
from contextlib import ExitStack

import concourse.bass as bass
from concourse import mybir

F32 = mybir.dt.float32
F32R = mybir.dt.float32r
ACT = mybir.ActivationFunctionType
ALU = mybir.AluOpType
AX_X = mybir.AxisListType.X

P = 128
QUAD = 32
QUADS = P // QUAD
ROWS = 512
GROUPS = ROWS // QUAD
TILES = ROWS // P
CHUNK_SLICES = 8
RING = 4
BATCH = 4
SPLITS = BATCH - 1
TURNED = 4
PARTS = 2
LN_EPS = 1e-5
OVERFLOW_MARGIN = 1e-8
ALPHA = 0.1


def bass_adj_resnorm(nc, x, adj, h, w, b, out):
    N, F = x.shape
    assert F == P and N % (QUADS * QUAD * CHUNK_SLICES) == 0
    QCOLS = N // QUADS
    SLICES = QCOLS // QUAD
    CHUNKS = SLICES // CHUNK_SLICES
    CCOLS = CHUNK_SLICES * QUAD
    BATCHES = SLICES // BATCH
    PER_CHUNK = CHUNK_SLICES // BATCH
    BLOCKS = N // ROWS
    PAIRS = BLOCKS // 2
    PIECE = CHUNK_SLICES
    PIECES = CHUNKS
    assert CHUNKS % RING == 0 and BATCHES % TURNED == 0 and BLOCKS % 2 == 0 and PER_CHUNK == 2
    FULLS = SLICES // BATCH
    SLOT_USES = CHUNKS // RING
    LOAD = 16 * QUADS

    def by_vector(k):
        return k % 2 == 0

    adj_v = adj.rearrange("(k g r) c -> k r g c", g=GROUPS, r=QUAD)
    x_v = x.rearrange("(k t p) f -> k p t f", t=TILES, p=P)
    h_v = h.rearrange("(k t p) f -> k p t f", t=TILES, p=P)
    out_v = out.rearrange("(k t p) f -> k p t f", t=TILES, p=P)
    x1_d = nc.dram_tensor("x1_scratch", (N, F), F32).ap()
    y_d = nc.dram_tensor("y_scratch", (N, F), F32).ap()
    x1_v = x1_d.rearrange("(k t p) f -> k p t f", t=TILES, p=P)
    y_v = y_d.rearrange("(k t p) f -> k p t f", t=TILES, p=P)

    with ExitStack() as ctx:
        def sb(name, shape, dt=F32):
            return ctx.enter_context(nc.sbuf_tensor(name, shape, dt))

        def psum(name, shape):
            return ctx.enter_context(nc.psum_tensor(name, shape, F32))

        def sem(name):
            return ctx.enter_context(nc.semaphore(name))

        adj_in = sb("adj_in", [P, RING, GROUPS, CCOLS])
        turned = [sb(f"turned{t}", [P, SPLITS if by_vector(t) else BATCH, ROWS]) for t in range(TURNED)]
        high = sb("high", [P, PARTS, SPLITS, ROWS], F32R)
        low = sb("low", [P, PARTS, SPLITS, ROWS], F32R)
        op_full = sb("op_full", [P, FULLS, F])
        op_split = sb("op_split", [P, FULLS * SPLITS, 2, F], F32R)
        stage = sb("stage", [P, 2, PIECE, F])
        x_sum = sb("x_sum", [P, 2, PIECE])
        acc_sb = sb("acc_sb", [P, ROWS])
        resid = sb("resid", [P, TILES, F])
        h_nat = sb("h_nat", [P, TILES, F])
        xh = sb("xh", [P, TILES, F])
        pre = sb("pre", [P, TILES, F])
        normed = sb("normed", [P, TILES, F])
        x1T = sb("x1T", [P, ROWS])
        fc = sb("fc", [P, TILES, F])
        y = sb("y", [P, TILES, F])
        junk = sb("junk", [P, TILES, F])
        w_sb = sb("w_sb", [P, F])
        b_sb = sb("b_sb", [P, F])
        ident = sb("ident", [P, P])
        eps_sb = sb("eps_sb", [P, 1])
        last_col = sb("last_col", [P, TILES])
        deg_root = sb("deg_root", [P, TILES])
        dinv = sb("dinv", [P, TILES])
        dinv_all = sb("dinv_all", [P, BLOCKS * TILES])
        bn = sb("bn", [P, TILES, 6])
        fence = sb("fence", [P, 1])
        meanvar = sb("meanvar", [P, TILES, 2])
        std = sb("std", [P, TILES])
        rstd = sb("rstd", [P, TILES])
        shift = sb("shift", [P, TILES])

        acc = [psum(f"acc{i}", [P, ROWS]) for i in range(2)]
        turned_ps = [psum(f"turned_ps{i}", [P, ROWS]) for i in range(2)]
        nat = psum("nat", [P, TILES, F])
        x1T_ps = psum("x1T_ps", [P, ROWS])
        fc_ps = psum("fc_ps", [P, TILES, F])

        adj_loaded = [sem(f"adj_loaded{s}") for s in range(RING)]
        op_loaded = [sem(f"op_loaded{s}") for s in range(2)]
        const_loaded = sem("const_loaded")
        ident_zero = sem("ident_zero")
        ident_ready = sem("ident_ready")
        eps_ready = sem("eps_ready")
        x_summed = sem("x_summed")
        x_shift_ready = sem("x_shift_ready")
        x_shifted = sem("x_shifted")
        x_centred = sem("x_centred")
        op_high = sem("op_high")
        op_full_ready = sem("op_full_ready")
        x_low = sem("x_low")
        y_low = sem("y_low")
        turned_ready = sem("turned_ready")
        turned_ps_ready = sem("turned_ps_ready")
        high_ready = sem("high_ready")
        high_ps_ready = sem("high_ps_ready")
        low_ready = sem("low_ready")
        low_ps_ready = sem("low_ps_ready")
        highs_used = sem("highs_used")
        multiplied = sem("multiplied")
        acc_copied = sem("acc_copied")
        nat_ready = sem("nat_ready")
        resid_loaded = sem("resid_loaded")
        h_loaded = sem("h_loaded")
        last_col_ready = sem("last_col_ready")
        xh_ready = sem("xh_ready")
        dinv_cur = sem("dinv_cur")
        scaled = sem("scaled")
        pre_ready = sem("pre_ready")
        deg_shift = sem("deg_shift")
        dinv_ready = sem("dinv_ready")
        dinv_kept = sem("dinv_kept")
        bn_ready = sem("bn_ready")
        stats_ready = sem("stats_ready")
        std_ready = sem("std_ready")
        rstd_ready = sem("rstd_ready")
        shift_ready = sem("shift_ready")
        normed_ready = sem("normed_ready")
        normed_stored = sem("normed_stored")
        x1T_ready = sem("x1T_ready")
        x1T_copied = sem("x1T_copied")
        fc_done = sem("fc_done")
        fc_ready = sem("fc_ready")
        y_ready = sem("y_ready")
        y_stored = sem("y_stored")

        def walk(eng, pair):
            pair(0, 1, None)
            with eng.Fori(1, PAIRS) as i:
                pair(i, 1, 1)
            pair(PAIRS, 2, 1)
            with eng.Fori(PAIRS + 1, 2 * PAIRS - 1) as i:
                pair(i, 2, 2)
            pair(2 * PAIRS - 1, 2, 2)

        def load_adj(eng, quads, block, c):
            for a in quads:
                cols = slice(a * QCOLS + c * CCOLS, a * QCOLS + (c + 1) * CCOLS)
                eng.dma_start(adj_in[a * QUAD:(a + 1) * QUAD, c % RING, :, :],
                              adj_v[block, :, :, cols]).then_inc(adj_loaded[c % RING], 16)

        block = ctx.enter_context(nc.Block())

        @block.sync
        def _(sp):
            def load_op(source, piece):
                q = piece % PIECES
                if piece >= 2:
                    sp.wait_ge(op_full_ready, piece - 1)
                    if piece - 2 < PIECES:
                        sp.wait_ge(x_low, piece - 1)
                    else:
                        sp.wait_ge(y_low, piece - 1 - PIECES)
                for a in range(QUADS):
                    rows = slice(a * QCOLS + q * PIECE * QUAD, a * QCOLS + (q + 1) * PIECE * QUAD)
                    sp.dma_start(stage[a * QUAD:(a + 1) * QUAD, q % 2, :, :],
                                 source[rows, :].rearrange("(s c) f -> c s f", c=QUAD)
                                 ).then_inc(op_loaded[q % 2], 16)

            def load_y(q):
                sp.wait_ge(y_stored, 16 * (BLOCKS - BLOCKS // QUADS + (q * CCOLS) // ROWS + 1))
                load_op(y_d, PIECES + q)

            def pair(i, layer, before):
                for par in range(2):
                    g = 2 * i + par
                    blk = g if layer == 1 else g - BLOCKS
                    peeled = before != layer and par == 0
                    for c in range(CHUNKS):
                        if not (peeled and layer == 1 and c < RING):
                            sp.wait_ge(turned_ready, g * BATCHES + PER_CHUNK * (c - RING + 1))
                            if peeled and layer == 1:
                                load_op(x, c)
                        if peeled and layer == 2 and c == 0:
                            load_y(0)
                            load_y(1)
                        if peeled and layer == 2 and c >= RING:
                            load_y(c - 2)
                        load_adj(sp, (0, 1), blk, c)
                        if peeled and layer == 1 and c == RING - 1:
                            load_op(x, 2)
                            load_op(x, 3)
                        if peeled and layer == 1 and c == 0:
                            sp.dma_start(w_sb[:, :], w).then_inc(const_loaded, 16)
                            sp.dma_start(b_sb[:, :], b.rearrange("(a n) -> a n", a=1).to_broadcast((P, F))
                                         ).then_inc(const_loaded, 16)
                        if peeled and layer == 2 and c == CHUNKS - 1:
                            load_y(PIECES - 2)
                            load_y(PIECES - 1)
                        if c == CHUNKS - 2:
                            if not (peeled and layer == 1):
                                sp.wait_ge(pre_ready, g)
                            if layer == 1:
                                sp.dma_start(resid[:, :, :], x_v[blk]).then_inc(resid_loaded, 16)
                                sp.dma_start(h_nat[:, :, :], h_v[blk]).then_inc(h_loaded, 16)
                            else:
                                sp.wait_ge(normed_stored, 16 * (blk + 1))
                                sp.dma_start(resid[:, :, :], x1_v[blk]).then_inc(resid_loaded, 16)

            load_op(x, 0)
            load_op(x, 1)
            walk(sp, pair)
            sp.wait_ge(normed_stored, 16 * 2 * BLOCKS)

        @block.vector
        def _(dve):
            def centre(q):
                s = q % 2
                dve.wait_ge(op_loaded[s], 16 * QUADS * (q // 2 + 1))
                nc.vector.tensor_reduce(x_sum[:, s, :], stage[:, s, :, :], AX_X, ALU.add).then_inc(x_summed, 1)
                dve.wait_ge(x_summed, q + 1)
                nc.vector.tensor_scalar(x_sum[:, s, :], x_sum[:, s, :], -1.0 / F, None,
                                        ALU.mult).then_inc(x_shift_ready, 1)
                dve.wait_ge(x_shift_ready, q + 1)
                nc.vector.tensor_tensor(stage[:, s, :, :], stage[:, s, :, :],
                                        x_sum[:, s, :].unsqueeze(2).to_broadcast((P, PIECE, F)),
                                        ALU.add).then_inc(x_shifted, 1)
                dve.wait_ge(x_shifted, q + 1)
                nc.vector.memset(stage[:, s, :, F - 1], 1.0).then_inc(x_centred, 1)

            def finish(k, g, layer):
                if k == 4 and layer == 1:
                    dve.wait_ge(resid_loaded, 16 * (g + 1))
                    dve.wait_ge(h_loaded, 16 * (g + 1))
                    nc.vector.scalar_tensor_tensor(xh[:, :, :], h_nat[:, :, :], ALPHA, resid[:, :, :],
                                                   ALU.mult, ALU.add).then_inc(xh_ready, 1)
                    dve.wait_ge(xh_ready, g + 1)
                    dve.wait_ge(last_col_ready, g + 1)
                    nc.vector.scalar_tensor_tensor(pre[:, :, 0:F - 1], nat[:, :, 0:F - 1], 1.0 - ALPHA,
                                                   xh[:, :, 0:F - 1], ALU.mult, ALU.add)
                    nc.vector.scalar_tensor_tensor(pre[:, :, F - 1], last_col[:, :], 1.0 - ALPHA,
                                                   xh[:, :, F - 1], ALU.mult, ALU.add).then_inc(pre_ready, 1)
                    nc.vector.tensor_scalar(deg_root[:, :], deg_root[:, :], OVERFLOW_MARGIN, None,
                                            ALU.add).then_inc(deg_shift, 1)
                    dve.wait_ge(deg_shift, g + 1)
                    nc.vector.reciprocal(dinv[:, :], deg_root[:, :]).then_inc(dinv_ready, 1)
                    dve.wait_ge(dinv_ready, g + 1)
                    nc.vector.tensor_copy(dinv_all[:, bass.ts(g, TILES)], dinv[:, :]).then_inc(dinv_kept, 1)
                if k == 4 and layer == 2:
                    dve.wait_ge(resid_loaded, 16 * (g + 1))
                    dve.wait_ge(scaled, g - BLOCKS + 1)
                    nc.vector.tensor_tensor(pre[:, :, :], xh[:, :, :], resid[:, :, :],
                                            ALU.add).then_inc(pre_ready, 1)
                if k == 5:
                    dve.wait_ge(pre_ready, g + 1)
                    for t in range(TILES):
                        last = nc.vector.bn_stats(bn[:, t, :], pre[:, t, :])
                    last.then_inc(bn_ready, 1)
                    dve.wait_ge(bn_ready, g + 1)
                    nc.vector.tensor_copy(fence[:, :], bn[:, 0, 0:1])
                    for t in range(TILES):
                        last = nc.vector.bn_aggr(meanvar[:, t, :], bn[:, t, :])
                    last.then_inc(stats_ready, 1)
                if k == 6:
                    dve.wait_ge(std_ready, g + 1)
                    nc.vector.reciprocal(rstd[:, :], std[:, :]).then_inc(rstd_ready, 1)
                    dve.wait_ge(rstd_ready, g + 1)
                    nc.vector.scalar_tensor_tensor(shift[:, :], meanvar[:, :, 0], -1.0, rstd[:, :],
                                                   ALU.mult, ALU.mult).then_inc(shift_ready, 1)
                if k == 10 and layer == 1:
                    dve.wait_ge(fc_done, g + 1)
                    nc.vector.tensor_tensor(fc[:, :, :], fc_ps[:, :, :],
                                            b_sb[:, :].unsqueeze(1).to_broadcast((P, TILES, F)),
                                            ALU.add).then_inc(fc_ready, 1)

            def y_low_part(q):
                dve.wait_ge(op_high, PIECES + q + 1)
                splits = slice(q * PER_CHUNK * SPLITS, (q + 1) * PER_CHUNK * SPLITS)
                lows = op_split[:, splits, 1, :].rearrange("p (k s) f -> p k s f", s=SPLITS)
                highs = op_split[:, splits, 0, :].bitcast(F32).rearrange("p (k s) f -> p k s f", s=SPLITS)
                raws = stage[:, q % 2, :, :].rearrange("p (k s) f -> p k s f", s=BATCH)[:, :, 1:BATCH, :]
                nc.vector.tensor_tensor(lows, raws, highs, ALU.subtract).then_inc(y_low, 1)

            def low_of_psum(n, k, even):
                dve.wait_ge(high_ps_ready, even + 1)
                if not (isinstance(n, int) and n < PARTS):
                    dve.wait_ge(multiplied, n - PARTS + 1)
                nc.vector.tensor_tensor(low[:, k % PARTS, SPLITS - 1, :], turned_ps[k // 2 % 2][:, :],
                                        high[:, k % PARTS, SPLITS - 1, :].bitcast(F32),
                                        ALU.subtract).then_inc(low_ps_ready, 1)

            def pair(i, layer, before):
                for par in range(2):
                    g = 2 * i + par
                    first = before is None and par == 0
                    first_of_2 = before is not None and before != layer and par == 0
                    for k in range(BATCHES):
                        n = g * BATCHES + k
                        even = g * (BATCHES // 2) + k // 2
                        c = k // PER_CHUNK
                        if k % PER_CHUNK == 0:
                            use = g * SLOT_USES + c // RING + 1
                            dve.wait_ge(adj_loaded[c % RING], use * LOAD)
                        if not (first and k < TURNED):
                            dve.wait_ge(highs_used, n - TURNED + 1)
                            dve.wait_ge(low_ready, n - TURNED + 1)
                        s0 = k % PER_CHUNK * BATCH
                        m = BATCH - 1 if by_vector(k) else BATCH
                        view = adj_in[:, c % RING, :, :].rearrange("p g (s c) -> p s g c", c=QUAD)
                        nc.vector.transpose(
                            turned[k % TURNED][:, :, :].rearrange("p s (g r) -> p s g r", r=QUAD),
                            view[:, s0:s0 + m, :, :]).then_inc(turned_ready, 1)
                        if by_vector(k):
                            nc.vector.transpose(turned_ps[k // 2 % 2][:, :].rearrange("p (g r) -> p g r", r=QUAD),
                                                view[:, s0 + m, :, :]).then_inc(turned_ps_ready, 1)
                        else:
                            low_of_psum(n - 1, k - 1, even)
                        if first_of_2 and k % PER_CHUNK == 0:
                            y_low_part(k // PER_CHUNK)
                        if first and k % 2 == 1 and 2 + k // 2 < PIECES:
                            centre(2 + k // 2)
                        if par == 1:
                            finish(k, g - 1, layer)
                        elif before is not None:
                            finish(k, g - 1, before)

            nc.vector.memset(eps_sb[:, :], LN_EPS).then_inc(eps_ready, 1)
            centre(0)
            centre(1)
            walk(dve, pair)
            for k in range(BATCHES):
                finish(k, 2 * BLOCKS - 1, 2)

        @block.scalar
        def _(act):
            def prepare(piece):
                s, q = piece % 2, piece % PIECES
                if piece < PIECES:
                    act.wait_ge(x_centred, q + 1)
                else:
                    act.wait_ge(op_loaded[s], 16 * QUADS * (piece // 2 + 1))
                    act.wait_ge(multiplied, (BLOCKS - 1) * BATCHES + PER_CHUNK * (q + 1))
                view = stage[:, s, :, :].rearrange("p (k s) f -> p k s f", s=BATCH)
                nc.scalar.copy(op_full[:, q * PER_CHUNK:(q + 1) * PER_CHUNK, :], view[:, :, 0, :]).then_inc(op_full_ready, 1)
                splits = slice(q * PER_CHUNK * SPLITS, (q + 1) * PER_CHUNK * SPLITS)
                nc.scalar.copy(op_split[:, splits, 0, :].rearrange("p (k s) f -> p k s f", s=SPLITS),
                               view[:, :, 1:BATCH, :]).then_inc(op_high, 1)

            def finish(k, g, layer, par):
                if k == 1:
                    act.wait_ge(multiplied, (g + 1) * BATCHES)
                    nc.scalar.copy(acc_sb[:, :], acc[par][:, :]).then_inc(acc_copied, 1)
                if k == 3:
                    act.wait_ge(nat_ready, g + 1)
                if k == 3 and layer == 1:
                    for t in range(TILES):
                        nc.scalar.activation(junk[:, t, 0:F - 1], nat[:, t, 0:F - 1], ACT.Copy, scale=-1.0,
                                             accum_out=last_col[:, t:t + 1])
                    nc.scalar.activation(deg_root[:, :], nat[:, :, F - 1], ACT.Sqrt).then_inc(last_col_ready, 1)
                if k == 3 and layer == 2:
                    nc.scalar.copy(dinv[:, :], dinv_all[:, bass.ts(g - BLOCKS, TILES)]).then_inc(dinv_cur, 1)
                    act.wait_ge(dinv_cur, g - BLOCKS + 1)
                    for t in range(TILES):
                        last = nc.scalar.activation(xh[:, t, :], nat[:, t, :], ACT.Copy, scale=dinv[:, t:t + 1])
                    last.then_inc(scaled, 1)
                if k == 5:
                    act.wait_ge(stats_ready, g + 1)
                    nc.scalar.activation(std[:, :], meanvar[:, :, 1], ACT.Sqrt,
                                         bias=eps_sb[:, 0:1]).then_inc(std_ready, 1)
                if k == 6:
                    act.wait_ge(shift_ready, g + 1)
                    if not (isinstance(g, int) and g == 0):
                        act.wait_ge(normed_stored, 16 * g)
                    for t in range(TILES):
                        last = nc.scalar.activation(normed[:, t, :], pre[:, t, :], ACT.Identity,
                                                    bias=shift[:, t:t + 1], scale=rstd[:, t:t + 1])
                    last.then_inc(normed_ready, 1)
                    act.wait_ge(normed_ready, g + 1)
                    rows = x1_v[g] if layer == 1 else out_v[g - BLOCKS]
                    act.dma_start(rows, normed[:, :, :]).then_inc(normed_stored, 16)
                if k == 8 and layer == 1:
                    act.wait_ge(x1T_ready, g + 1)
                    nc.scalar.copy(x1T[:, :], x1T_ps[:, :]).then_inc(x1T_copied, 1)
                if k == 10 and layer == 1:
                    act.wait_ge(fc_ready, g + 1)
                    if not (isinstance(g, int) and g == 0):
                        act.wait_ge(y_stored, 16 * g)
                    for t in range(TILES):
                        last = nc.scalar.activation(y[:, t, :], fc[:, t, :], ACT.Copy, scale=dinv[:, t:t + 1])
                    last.then_inc(y_ready, 1)
                    act.wait_ge(y_ready, g + 1)
                    act.dma_start(y_v[g], y[:, :, :]).then_inc(y_stored, 16)

            def pair(i, layer, before):
                for par in range(2):
                    g = 2 * i + par
                    blk = g if layer == 1 else g - BLOCKS
                    first = before is None and par == 0
                    first_of_2 = before is not None and before != layer and par == 0
                    for k in range(BATCHES):
                        n = g * BATCHES + k
                        even = g * (BATCHES // 2) + k // 2
                        parts = slice(0, SPLITS - 1 if by_vector(k) else SPLITS)
                        if first_of_2 and (k == 0 or k % PER_CHUNK == 1 and k // PER_CHUNK + 1 < PIECES):
                            prepare(PIECES + (k + 1) // PER_CHUNK)
                        if not (first and k < PARTS):
                            act.wait_ge(highs_used, n - PARTS + 1)
                            act.wait_ge(low_ready, n - PARTS + 1)
                            if by_vector(k):
                                act.wait_ge(low_ps_ready, even)
                        act.wait_ge(turned_ready, n + 1)
                        nc.scalar.copy(high[:, k % PARTS, parts, :],
                                       turned[k % TURNED][:, 1:, :]).then_inc(high_ready, 1)
                        if by_vector(k):
                            act.wait_ge(turned_ps_ready, even + 1)
                            nc.scalar.copy(high[:, k % PARTS, SPLITS - 1, :],
                                           turned_ps[k // 2 % 2][:, :]).then_inc(high_ps_ready, 1)
                        if first and k % 2 == 1 and 2 + k // 2 < PIECES:
                            prepare(2 + k // 2)
                        if k % PER_CHUNK == PER_CHUNK - 1:
                            c = k // PER_CHUNK + RING
                            if c < CHUNKS:
                                load_adj(act, (2, 3), blk, c)
                            elif not (isinstance(i, int) and i == 2 * PAIRS - 1 and par == 1):
                                load_adj(act, (2, 3), (g + 1) % BLOCKS, c - CHUNKS)
                        if par == 1:
                            finish(k, g - 1, layer, 0)
                        elif before is not None:
                            finish(k, g - 1, before, 1)

            for c in range(RING):
                load_adj(act, (2, 3), 0, c)
            act.wait_ge(eps_ready, 1)
            prepare(0)
            prepare(1)
            walk(act, pair)
            for k in range(BATCHES):
                finish(k, 2 * BLOCKS - 1, 2, 1)

        @block.gpsimd
        def _(pool):
            def prepare(q):
                s = q % 2
                pool.wait_ge(op_high, q + 1)
                splits = slice(q * PER_CHUNK * SPLITS, (q + 1) * PER_CHUNK * SPLITS)
                view = op_split[:, splits, :, :].rearrange("p (k s) h f -> p k s h f", s=SPLITS)
                for k in range(PER_CHUNK):
                    last = nc.gpsimd.tensor_tensor(view[:, k, :, 1, :],
                                                   stage[:, s, k * BATCH + 1:(k + 1) * BATCH, :],
                                                   view[:, k, :, 0, :].bitcast(F32), ALU.subtract)
                last.then_inc(x_low, 1)

            def pair(i, layer, before):
                for par in range(2):
                    g = 2 * i + par
                    first = before is None and par == 0
                    first_of_2 = before is not None and before != layer and par == 0
                    for k in range(BATCHES):
                        n = g * BATCHES + k
                        parts = slice(0, SPLITS - 1 if by_vector(k) else SPLITS)
                        pool.wait_ge(high_ready, n + 1)
                        if not (first and k < PARTS):
                            pool.wait_ge(multiplied, n - PARTS + 1)
                        nc.gpsimd.tensor_tensor(low[:, k % PARTS, parts, :], turned[k % TURNED][:, 1:, :],
                                                high[:, k % PARTS, parts, :].bitcast(F32),
                                                ALU.subtract).then_inc(low_ready, 1)
                        if first and k % 2 == 1 and 2 + k // 2 < PIECES:
                            prepare(2 + k // 2)

            nc.gpsimd.memset(ident[:, :], 0.0).then_inc(ident_zero, 1)
            pool.wait_ge(ident_zero, 1)
            nc.gpsimd.affine_select(out=ident[:, :], in_=ident[:, :], compare_op=ALU.not_equal, fill=1.0, base=0,
                                    pattern=[[-1, P]], channel_multiplier=1).then_inc(ident_ready, 1)
            prepare(0)
            prepare(1)
            walk(pool, pair)

        @block.tensor
        def _(pe):
            def finish(k, g, layer):
                if k == 1:
                    pe.wait_ge(acc_copied, g + 1)
                    for t in range(TILES):
                        last = nc.tensor.transpose(nat[:, t, :], acc_sb[:, t * P:(t + 1) * P], ident[:, :])
                    last.then_inc(nat_ready, 1)
                if k == 6 and layer == 1:
                    pe.wait_ge(normed_ready, g + 1)
                    for t in range(TILES):
                        last = nc.tensor.transpose(x1T_ps[:, t * P:(t + 1) * P], normed[:, t, :], ident[:, :])
                    last.then_inc(x1T_ready, 1)
                if k == 8 and layer == 1:
                    pe.wait_ge(x1T_copied, g + 1)
                    for t in range(TILES):
                        last = nc.tensor.matmul(fc_ps[:, t, :], x1T[:, t * P:(t + 1) * P], w_sb[:, :],
                                                start=True, stop=True)
                    last.then_inc(fc_done, 1)

            def highs(n, k, even, to):
                pe.wait_ge(turned_ready, n + 1)
                nc.tensor.matmul(to, op_full[:, k, :], turned[k % TURNED][:, 0, :], start=k == 0, stop=False)
                pe.wait_ge(high_ready, n + 1)
                for s in range(SPLITS):
                    if s == SPLITS - 1 and by_vector(k):
                        pe.wait_ge(high_ps_ready, even + 1)
                    for part in (1, 0):
                        last = nc.tensor.matmul(to, op_split[:, k * SPLITS + s, part, :], high[:, k % PARTS, s, :],
                                                start=False, stop=False)
                last.then_inc(highs_used, 1)

            def lows(n, k, even, to):
                pe.wait_ge(low_ready, n + 1)
                for s in range(SPLITS):
                    if s == SPLITS - 1 and by_vector(k):
                        pe.wait_ge(low_ps_ready, even + 1)
                    last = nc.tensor.matmul(to, op_split[:, k * SPLITS + s, 0, :], low[:, k % PARTS, s, :],
                                            start=False, stop=k == BATCHES - 1 and s == SPLITS - 1)
                last.then_inc(multiplied, 1)

            def pair(i, layer, before):
                for par in range(2):
                    g = 2 * i + par
                    first = before is None and par == 0
                    first_of_2 = before is not None and before != layer and par == 0
                    for k in range(BATCHES):
                        n = g * BATCHES + k
                        even = g * (BATCHES // 2) + k // 2
                        if first and k % PER_CHUNK == 0:
                            pe.wait_ge(op_full_ready, k // PER_CHUNK + 1)
                            pe.wait_ge(x_low, k // PER_CHUNK + 1)
                        if first_of_2 and k % PER_CHUNK == 0:
                            pe.wait_ge(op_full_ready, PIECES + k // PER_CHUNK + 1)
                            pe.wait_ge(y_low, k // PER_CHUNK + 1)
                        highs(n, k, even, acc[par][:, :])
                        if k > 0:
                            lows(n - 1, k - 1, even, acc[par][:, :])
                        elif not first:
                            lows(n - 1, BATCHES - 1, even - 1, acc[1 - par][:, :])
                        if par == 1:
                            finish(k, g - 1, layer)
                        elif before is not None:
                            finish(k, g - 1, before)

            pe.wait_ge(ident_ready, 1)
            pe.wait_ge(const_loaded, 32)
            walk(pe, pair)
            lows(2 * BLOCKS * BATCHES - 1, BATCHES - 1, 0, acc[1][:, :])
            for k in range(BATCHES):
                finish(k, 2 * BLOCKS - 1, 2)


_INS = ['x', 'adj', 'L0_gnn_h', 'L1_gnn_W', 'L1_gnn_b']


def kernel(**inputs):
    import numpy as _np
    import concourse.bacc as _bacc
    from concourse import mybir as _mybir
    from concourse.bass_utils import run_bass_kernel_spmd as _run

    nc = _bacc.Bacc("TRN2", target_bir_lowering=False, num_devices=1)
    arrays, args = {}, []
    for name in _INS:
        a = _np.ascontiguousarray(inputs[name])
        arrays[f"in_{name}_dram"] = a
        args.append(nc.dram_tensor(f"in_{name}_dram", a.shape, _mybir.dt.from_np(a.dtype), kind="ExternalInput").ap())
    out = nc.dram_tensor("out_0_dram", inputs["x"].shape, _mybir.dt.float32, kind="ExternalOutput").ap()
    bass_adj_resnorm(nc, *args, out)
    r = _run(nc, [arrays], core_ids=[0])
    return r.results[0]["out_0_dram"]
```

```python
from contextlib import ExitStack

import concourse.bass as bass
from concourse import mybir

F32 = mybir.dt.float32
F32R = mybir.dt.float32r
ACT = mybir.ActivationFunctionType
ALU = mybir.AluOpType
AX_X = mybir.AxisListType.X

P = 128
QUAD = 32
QUADS = P // QUAD
ROWS = 512
GROUPS = ROWS // QUAD
TILES = ROWS // P
CHUNK_SLICES = 8
RING = 4
BATCH = 4
SPLITS = BATCH - 1
TURNED = 4
PARTS = 2
LN_EPS = 1e-5
OVERFLOW_MARGIN = 1e-8
ALPHA = 0.1


def bass_adj_resnorm(nc, x, adj, h, w, b, out):
    N, F = x.shape
    assert F == P and N % (QUADS * QUAD * CHUNK_SLICES) == 0
    QCOLS = N // QUADS
    SLICES = QCOLS // QUAD
    CHUNKS = SLICES // CHUNK_SLICES
    CCOLS = CHUNK_SLICES * QUAD
    BATCHES = SLICES // BATCH
    PER_CHUNK = CHUNK_SLICES // BATCH
    BLOCKS = N // ROWS
    PAIRS = BLOCKS // 2
    PIECE = CHUNK_SLICES
    PIECES = CHUNKS
    assert CHUNKS % RING == 0 and BATCHES % TURNED == 0 and BLOCKS % 2 == 0 and PER_CHUNK == 2
    FULLS = SLICES // BATCH
    SLOT_USES = CHUNKS // RING
    LOAD = 16 * QUADS

    HELD = RING // 2
    TURN_ORDER = [*range(CHUNKS - RING, CHUNKS - HELD), *range(CHUNKS - RING), *range(CHUNKS - HELD, CHUNKS)]

    def chunk_at(p, turn):
        return TURN_ORDER[p] if turn else p

    def slot_at(p, turn):
        if not turn:
            return p % RING
        return p % HELD if p < CHUNKS - HELD else p % RING

    def batch_at(k, turn):
        return chunk_at(k // PER_CHUNK, turn) * PER_CHUNK + k % PER_CHUNK

    KEPT = PAIRS - 1

    def kept_at(i, par, layer, before):
        if par == 0 and layer == 1 and before == 1:
            return i - 1
        if par == 1 and layer == 2 and before == 2:
            return i - PAIRS - 1
        return None

    def rows_of(g, layer):
        if layer == 1:
            return g
        return BLOCKS - 1 if isinstance(g, int) and g == BLOCKS else g - BLOCKS - 1

    def by_vector(k):
        return k % 2 == 0

    adj_v = adj.rearrange("(k g r) c -> k r g c", g=GROUPS, r=QUAD)
    x_v = x.rearrange("(k p t) f -> k p t f", t=TILES, p=P)
    h_v = h.rearrange("(k p t) f -> k p t f", t=TILES, p=P)
    out_v = out.rearrange("(k p t) f -> k p t f", t=TILES, p=P)
    x1_d = nc.dram_tensor("x1_scratch", (N, F), F32).ap()
    y_d = nc.dram_tensor("y_scratch", (N, F), F32).ap()
    x1_v = x1_d.rearrange("(k p t) f -> k p t f", t=TILES, p=P)
    y_v = y_d.rearrange("(k p t) f -> k p t f", t=TILES, p=P)

    with ExitStack() as ctx:
        def sb(name, shape, dt=F32):
            return ctx.enter_context(nc.sbuf_tensor(name, shape, dt))

        def psum(name, shape):
            return ctx.enter_context(nc.psum_tensor(name, shape, F32))

        def sem(name):
            return ctx.enter_context(nc.semaphore(name))

        adj_in = sb("adj_in", [P, RING, GROUPS, CCOLS])
        turned = [sb(f"turned{t}", [P, SPLITS if by_vector(t) else BATCH, ROWS]) for t in range(TURNED)]
        high = sb("high", [P, PARTS, SPLITS, ROWS], F32R)
        low = sb("low", [P, PARTS, SPLITS, ROWS], F32R)
        op_full = sb("op_full", [P, FULLS, F])
        op_split = sb("op_split", [P, FULLS * SPLITS, 2, F], F32R)
        stage = sb("stage", [P, 2, PIECE, F])
        x_sum = sb("x_sum", [P, 2, PIECE])
        acc_sb = sb("acc_sb", [P, ROWS])
        resid = sb("resid", [P, TILES, F])
        pre = sb("pre", [P, TILES, F])
        normed = sb("normed", [P, TILES, F])
        y = sb("y", [P, TILES, F])
        x1_kept = sb("x1_kept", [P, KEPT * TILES, F])
        w_sb = sb("w_sb", [P, F])
        b_sb = sb("b_sb", [P, F])
        ident = sb("ident", [P, P])
        eps_sb = sb("eps_sb", [P, 1])
        last_col = sb("last_col", [P, TILES])
        deg_root = sb("deg_root", [P, TILES])
        dinv = sb("dinv", [P, TILES])
        dinv_all = sb("dinv_all", [P, BLOCKS * TILES])
        bn = sb("bn", [P, TILES, 6])
        fence = sb("fence", [P, 1])
        meanvar = sb("meanvar", [P, TILES, 2])
        std = sb("std", [P, TILES])
        rstd = sb("rstd", [P, TILES])
        shift = sb("shift", [P, TILES])

        acc = [psum(f"acc{i}", [P, ROWS]) for i in range(2)]
        turned_ps = [psum(f"turned_ps{i}", [P, ROWS]) for i in range(2)]
        nat = psum("nat", [P, TILES, F])
        x1T_ps = psum("x1T_ps", [P, ROWS])
        fc_ps = psum("fc_ps", [P, TILES, F])

        acc_rows = acc_sb[:, :].rearrange("f (p t) -> f t p", t=TILES)

        adj_loaded = [sem(f"adj_loaded{s}") for s in range(RING)]
        op_loaded = [sem(f"op_loaded{s}") for s in range(2)]
        const_loaded = sem("const_loaded")
        ident_zero = sem("ident_zero")
        ident_ready = sem("ident_ready")
        eps_ready = sem("eps_ready")
        x_summed = sem("x_summed")
        x_shift_ready = sem("x_shift_ready")
        x_shifted = sem("x_shifted")
        x_centred = sem("x_centred")
        op_high = sem("op_high")
        op_full_ready = sem("op_full_ready")
        x_low = sem("x_low")
        y_low = sem("y_low")
        turned_ready = sem("turned_ready")
        turned_ps_ready = sem("turned_ps_ready")
        high_ready = sem("high_ready")
        high_ps_ready = sem("high_ps_ready")
        low_ready = sem("low_ready")
        low_ps_ready = sem("low_ps_ready")
        highs_used = sem("highs_used")
        multiplied = sem("multiplied")
        acc_copied = sem("acc_copied")
        nat_ready = sem("nat_ready")
        resid_loaded = sem("resid_loaded")
        h_loaded = sem("h_loaded")
        last_col_ready = sem("last_col_ready")
        xh_ready = sem("xh_ready")
        dinv_cur = sem("dinv_cur")
        scaled = sem("scaled")
        pre_ready = sem("pre_ready")
        deg_shift = sem("deg_shift")
        dinv_ready = sem("dinv_ready")
        dinv_kept = sem("dinv_kept")
        bn_ready = sem("bn_ready")
        stats_ready = sem("stats_ready")
        std_ready = sem("std_ready")
        rstd_ready = sem("rstd_ready")
        shift_ready = sem("shift_ready")
        normed_ready = sem("normed_ready")
        normed_stored = sem("normed_stored")
        x1_is_kept = sem("x1_is_kept")
        x1T_ready = sem("x1T_ready")
        x1T_copied = sem("x1T_copied")
        fc_done = sem("fc_done")
        fc_ready = sem("fc_ready")
        y_ready = sem("y_ready")
        y_stored = sem("y_stored")

        def walk(eng, pair):
            pair(0, 1, None)
            with eng.Fori(1, PAIRS - 1) as i:
                pair(i, 1, 1)
            pair(PAIRS - 1, 1, 1)
            pair(PAIRS, 2, 1)
            with eng.Fori(PAIRS + 1, 2 * PAIRS - 1) as i:
                pair(i, 2, 2)
            pair(2 * PAIRS - 1, 2, 2)

        def load_adj(eng, quads, rows, c, slot):
            for a in quads:
                cols = slice(a * QCOLS + c * CCOLS, a * QCOLS + (c + 1) * CCOLS)
                eng.dma_start(adj_in[a * QUAD:(a + 1) * QUAD, slot, :, :],
                              adj_v[rows, :, :, cols]).then_inc(adj_loaded[slot], 16)

        def load_stage(eng, source, p, q):
            for a in range(QUADS):
                rows = slice(a * QCOLS + q * PIECE * QUAD, a * QCOLS + (q + 1) * PIECE * QUAD)
                eng.dma_start(stage[a * QUAD:(a + 1) * QUAD, p % 2, :, :],
                              source[rows, :].rearrange("(s c) f -> c s f", c=QUAD)
                              ).then_inc(op_loaded[p % 2], 16)

        block = ctx.enter_context(nc.Block())

        @block.sync
        def _(sp):
            def load_op(source, p, q):
                sp.wait_ge(op_full_ready, p - 1)
                if p - 2 < PIECES:
                    sp.wait_ge(x_low, p - 1)
                else:
                    sp.wait_ge(y_low, p - 1 - PIECES)
                load_stage(sp, source, p, q)

            def load_y(p):
                q = chunk_at(p, True)
                sp.wait_ge(y_stored, 16 * (BLOCKS - BLOCKS // QUADS + (q * CCOLS) // ROWS + 1))
                load_op(y_d, PIECES + p, q)

            def load_chunk(g, rows, c):
                sp.wait_ge(turned_ready, g * BATCHES + PER_CHUNK * (c - RING + 1))
                load_adj(sp, (0, 1), rows, c, slot_at(c, False))

            def load_resid(g, rows, layer):
                if not (isinstance(g, int) and g == 0):
                    sp.wait_ge(pre_ready, g)
                if layer == 1:
                    sp.dma_start(resid[:, :, :], x_v[rows]).then_inc(resid_loaded, 16)
                    if not (isinstance(g, int) and g == 0):
                        sp.wait_ge(normed_ready, g)
                    sp.dma_start(pre[:, :, :], h_v[rows]).then_inc(h_loaded, 16)
                else:
                    if isinstance(g, int) and g == BLOCKS:
                        sp.wait_ge(normed_stored, 16 * (BLOCKS - KEPT))
                    sp.dma_start(resid[:, :, :], x1_v[rows]).then_inc(resid_loaded, 16)

            def first_block():
                load_stage(sp, x, 0, 0)
                load_adj(sp, (0, 1), 0, 0, 0)
                sp.dma_start(w_sb[:, :], w).then_inc(const_loaded, 16)
                sp.dma_start(b_sb[:, :], b.rearrange("(a n) -> a n", a=1).to_broadcast((P, F))
                             ).then_inc(const_loaded, 16)
                load_adj(sp, (0, 1), 0, 1, 1)
                for c in range(2, RING):
                    load_op(x, c, c)
                    load_adj(sp, (0, 1), 0, c, c)
                for c in range(RING, CHUNKS):
                    load_op(x, c, c)
                    load_chunk(0, 0, c)
                    if c == CHUNKS - 2:
                        load_resid(0, 0, 1)

            def turn_block():
                for p in range(HELD):
                    load_y(p)
                for p in range(HELD, CHUNKS - HELD):
                    load_y(p)
                    sp.wait_ge(turned_ready, BLOCKS * BATCHES + PER_CHUNK * (p - HELD + 1))
                    load_adj(sp, (0, 1), rows_of(BLOCKS, 2), chunk_at(p, True), slot_at(p, True))
                load_chunk(BLOCKS + 1, rows_of(BLOCKS + 1, 2), 0)
                for p in range(CHUNKS - HELD, CHUNKS):
                    load_y(p)
                load_resid(BLOCKS, rows_of(BLOCKS, 2), 2)

            def pair(i, layer, before):
                for par in range(2):
                    g = 2 * i + par
                    rows = rows_of(g, layer)
                    peeled = before != layer and par == 0
                    if peeled:
                        first_block() if layer == 1 else turn_block()
                        continue
                    for c in range(CHUNKS):
                        if not (before != layer and layer == 2 and c == 0):
                            load_chunk(g, rows, c)
                        if c == CHUNKS - 2 and (layer == 1 or par == 1):
                            load_resid(g, rows, layer)

            walk(sp, pair)
            sp.wait_ge(normed_stored, 16 * (2 * BLOCKS - KEPT))

        @block.vector
        def _(dve):
            def centre(q):
                s = q % 2
                dve.wait_ge(op_loaded[s], 16 * QUADS * (q // 2 + 1))
                nc.vector.tensor_reduce(x_sum[:, s, :], stage[:, s, :, :], AX_X, ALU.add).then_inc(x_summed, 1)
                dve.wait_ge(x_summed, q + 1)
                nc.vector.tensor_scalar(x_sum[:, s, :], x_sum[:, s, :], -1.0 / F, None,
                                        ALU.mult).then_inc(x_shift_ready, 1)
                dve.wait_ge(x_shift_ready, q + 1)
                nc.vector.tensor_tensor(stage[:, s, :, :], stage[:, s, :, :],
                                        x_sum[:, s, :].unsqueeze(2).to_broadcast((P, PIECE, F)),
                                        ALU.add).then_inc(x_shifted, 1)
                dve.wait_ge(x_shifted, q + 1)
                nc.vector.memset(stage[:, s, :, F - 1], 1.0).then_inc(x_centred, 1)

            def finish(k, g, layer, i, kept):
                if k == 4 and layer == 1:
                    dve.wait_ge(resid_loaded, 16 * (g + 1))
                    dve.wait_ge(h_loaded, 16 * (g + 1))
                    nc.vector.scalar_tensor_tensor(pre[:, :, :], pre[:, :, :], ALPHA, resid[:, :, :],
                                                   ALU.mult, ALU.add).then_inc(xh_ready, 1)
                    dve.wait_ge(xh_ready, g + 1)
                    dve.wait_ge(last_col_ready, g + 1)
                    nc.vector.scalar_tensor_tensor(pre[:, :, 0:F - 1], nat[:, :, 0:F - 1], 1.0 - ALPHA,
                                                   pre[:, :, 0:F - 1], ALU.mult, ALU.add)
                    nc.vector.scalar_tensor_tensor(pre[:, :, F - 1], last_col[:, :], 1.0 - ALPHA,
                                                   pre[:, :, F - 1], ALU.mult, ALU.add).then_inc(pre_ready, 1)
                    nc.vector.tensor_scalar(deg_root[:, :], deg_root[:, :], OVERFLOW_MARGIN, None,
                                            ALU.add).then_inc(deg_shift, 1)
                    dve.wait_ge(deg_shift, g + 1)
                    nc.vector.reciprocal(dinv[:, :], deg_root[:, :]).then_inc(dinv_ready, 1)
                    dve.wait_ge(dinv_ready, g + 1)
                    nc.vector.tensor_copy(dinv_all[:, bass.ts(g, TILES)], dinv[:, :]).then_inc(dinv_kept, 1)
                if k == 4 and layer == 2:
                    dve.wait_ge(scaled, g - BLOCKS + 1)
                    if kept is None:
                        dve.wait_ge(resid_loaded, 16 * (BLOCKS + 1 + i - PAIRS))
                        nc.vector.tensor_tensor(pre[:, :, :], pre[:, :, :], resid[:, :, :],
                                                ALU.add).then_inc(pre_ready, 1)
                    else:
                        dve.wait_ge(x1_is_kept, KEPT)
                        nc.vector.tensor_tensor(pre[:, :, :], pre[:, :, :], x1_kept[:, bass.ts(kept, TILES), :],
                                                ALU.add).then_inc(pre_ready, 1)
                if k == 5:
                    dve.wait_ge(pre_ready, g + 1)
                    for t in range(TILES):
                        last = nc.vector.bn_stats(bn[:, t, :], pre[:, t, :])
                    last.then_inc(bn_ready, 1)
                    dve.wait_ge(bn_ready, g + 1)
                    nc.vector.tensor_copy(fence[:, :], bn[:, 0, 0:1])
                    for t in range(TILES):
                        last = nc.vector.bn_aggr(meanvar[:, t, :], bn[:, t, :])
                    last.then_inc(stats_ready, 1)
                if k == 6:
                    dve.wait_ge(std_ready, g + 1)
                    nc.vector.reciprocal(rstd[:, :], std[:, :]).then_inc(rstd_ready, 1)
                    dve.wait_ge(rstd_ready, g + 1)
                    nc.vector.scalar_tensor_tensor(shift[:, :], meanvar[:, :, 0], -1.0, rstd[:, :],
                                                   ALU.mult, ALU.mult).then_inc(shift_ready, 1)
                if k == 9 and layer == 1:
                    dve.wait_ge(fc_done, g + 1)
                    nc.vector.tensor_tensor(y[:, :, :], fc_ps[:, :, :],
                                            b_sb[:, :].unsqueeze(1).to_broadcast((P, TILES, F)),
                                            ALU.add).then_inc(fc_ready, 1)

            def y_low_part(p):
                q = chunk_at(p, True)
                dve.wait_ge(op_high, PIECES + p + 1)
                splits = slice(q * PER_CHUNK * SPLITS, (q + 1) * PER_CHUNK * SPLITS)
                lows = op_split[:, splits, 1, :].rearrange("p (k s) f -> p k s f", s=SPLITS)
                highs = op_split[:, splits, 0, :].bitcast(F32).rearrange("p (k s) f -> p k s f", s=SPLITS)
                raws = stage[:, p % 2, :, :].rearrange("p (k s) f -> p k s f", s=BATCH)[:, :, 1:BATCH, :]
                nc.vector.tensor_tensor(lows, raws, highs, ALU.subtract).then_inc(y_low, 1)

            def low_of_psum(n, k, even):
                dve.wait_ge(high_ps_ready, even + 1)
                if not (isinstance(n, int) and n < PARTS):
                    dve.wait_ge(multiplied, n - PARTS + 1)
                nc.vector.tensor_tensor(low[:, k % PARTS, SPLITS - 1, :], turned_ps[k // 2 % 2][:, :],
                                        high[:, k % PARTS, SPLITS - 1, :].bitcast(F32),
                                        ALU.subtract).then_inc(low_ps_ready, 1)

            def pair(i, layer, before):
                for par in range(2):
                    g = 2 * i + par
                    first = before is None and par == 0
                    turn = before is not None and before != layer and par == 0
                    for k in range(BATCHES):
                        n = g * BATCHES + k
                        even = g * (BATCHES // 2) + k // 2
                        c = k // PER_CHUNK
                        slot = slot_at(c, turn)
                        if k % PER_CHUNK == 0 and not turn:
                            use = g * SLOT_USES + c // RING + 1
                            if layer == 2 and slot >= HELD:
                                use = use - SLOT_USES
                            dve.wait_ge(adj_loaded[slot], use * LOAD)
                        if k % PER_CHUNK == 0 and turn and HELD <= c < CHUNKS - HELD:
                            dve.wait_ge(adj_loaded[slot], (g * SLOT_USES + c // HELD) * LOAD)
                        if not (first and k < TURNED):
                            dve.wait_ge(highs_used, n - TURNED + 1)
                            dve.wait_ge(low_ready, n - TURNED + 1)
                        s0 = k % PER_CHUNK * BATCH
                        m = BATCH - 1 if by_vector(k) else BATCH
                        view = adj_in[:, slot, :, :].rearrange("p g (s c) -> p s g c", c=QUAD)
                        nc.vector.transpose(
                            turned[k % TURNED][:, :, :].rearrange("p s (g r) -> p s g r", r=QUAD),
                            view[:, s0:s0 + m, :, :]).then_inc(turned_ready, 1)
                        if by_vector(k):
                            nc.vector.transpose(turned_ps[k // 2 % 2][:, :].rearrange("p (g r) -> p g r", r=QUAD),
                                                view[:, s0 + m, :, :]).then_inc(turned_ps_ready, 1)
                        else:
                            low_of_psum(n - 1, k - 1, even)
                        if turn and k % PER_CHUNK == 0:
                            y_low_part(k // PER_CHUNK)
                        if first and k % 2 == 1 and 2 + k // 2 < PIECES:
                            centre(2 + k // 2)
                        if par == 1:
                            finish(k, g - 1, layer, i, kept_at(i, par, layer, before))
                        elif before is not None:
                            finish(k, g - 1, before, i, kept_at(i, par, layer, before))

            nc.vector.memset(eps_sb[:, :], LN_EPS).then_inc(eps_ready, 1)
            centre(0)
            centre(1)
            walk(dve, pair)
            for k in range(BATCHES):
                finish(k, 2 * BLOCKS - 1, 2, 2 * PAIRS, None)

        @block.scalar
        def _(act):
            def prepare(piece):
                s, q = piece % 2, chunk_at(piece % PIECES, piece >= PIECES)
                if piece < PIECES:
                    act.wait_ge(x_centred, piece + 1)
                else:
                    act.wait_ge(op_loaded[s], 16 * QUADS * (piece // 2 + 1))
                    act.wait_ge(multiplied, (BLOCKS - 1) * BATCHES + PER_CHUNK * (q + 1))
                view = stage[:, s, :, :].rearrange("p (k s) f -> p k s f", s=BATCH)
                nc.scalar.copy(op_full[:, q * PER_CHUNK:(q + 1) * PER_CHUNK, :], view[:, :, 0, :]).then_inc(op_full_ready, 1)
                splits = slice(q * PER_CHUNK * SPLITS, (q + 1) * PER_CHUNK * SPLITS)
                nc.scalar.copy(op_split[:, splits, 0, :].rearrange("p (k s) f -> p k s f", s=SPLITS),
                               view[:, :, 1:BATCH, :]).then_inc(op_high, 1)

            def finish(k, g, layer, par, i, kept):
                if k == 1:
                    act.wait_ge(multiplied, (g + 1) * BATCHES)
                    nc.scalar.copy(acc_sb[:, :], acc[par][:, :]).then_inc(acc_copied, 1)
                if k == 3:
                    act.wait_ge(nat_ready, g + 1)
                if k == 3 and layer == 1:
                    if not (isinstance(g, int) and g == 0):
                        act.wait_ge(y_stored, 16 * g)
                    for t in range(TILES):
                        nc.scalar.activation(y[:, t, 0:F - 1], nat[:, t, 0:F - 1], ACT.Copy, scale=-1.0,
                                             accum_out=last_col[:, t:t + 1])
                    nc.scalar.activation(deg_root[:, :], nat[:, :, F - 1], ACT.Sqrt).then_inc(last_col_ready, 1)
                if k == 3 and layer == 2:
                    act.wait_ge(dinv_kept, BLOCKS)
                    nc.scalar.copy(dinv[:, :], dinv_all[:, bass.ts(rows_of(g, 2), TILES)]).then_inc(dinv_cur, 1)
                    act.wait_ge(dinv_cur, g - BLOCKS + 1)
                    for t in range(TILES):
                        last = nc.scalar.activation(pre[:, t, :], nat[:, t, :], ACT.Copy, scale=dinv[:, t:t + 1])
                    last.then_inc(scaled, 1)
                if k == 5:
                    act.wait_ge(stats_ready, g + 1)
                    nc.scalar.activation(std[:, :], meanvar[:, :, 1], ACT.Sqrt,
                                         bias=eps_sb[:, 0:1]).then_inc(std_ready, 1)
                if k == 6:
                    act.wait_ge(shift_ready, g + 1)
                    if layer == 2:
                        act.wait_ge(normed_stored, 16 * (g - KEPT))
                    elif not (isinstance(i, int) and i == 0):
                        act.wait_ge(normed_stored, 16 * i)
                    for t in range(TILES):
                        last = nc.scalar.activation(normed[:, t, :], pre[:, t, :], ACT.Identity,
                                                    bias=shift[:, t:t + 1], scale=rstd[:, t:t + 1])
                    last.then_inc(normed_ready, 1)
                    act.wait_ge(normed_ready, g + 1)
                    if layer == 1 and kept is not None:
                        nc.scalar.copy(x1_kept[:, bass.ts(kept, TILES), :], normed[:, :, :]).then_inc(x1_is_kept, 1)
                    else:
                        rows = (x1_v if layer == 1 else out_v)[rows_of(g, layer)]
                        act.dma_start(rows, normed[:, :, :]).then_inc(normed_stored, 16)
                if k == 7 and layer == 1:
                    act.wait_ge(x1T_ready, g + 1)
                    nc.scalar.copy(acc_sb[:, :], x1T_ps[:, :]).then_inc(x1T_copied, 1)
                if k == 9 and layer == 1:
                    act.wait_ge(fc_ready, g + 1)
                    for t in range(TILES):
                        last = nc.scalar.activation(y[:, t, :], y[:, t, :], ACT.Copy, scale=dinv[:, t:t + 1])
                    last.then_inc(y_ready, 1)
                    act.wait_ge(y_ready, g + 1)
                    act.dma_start(y_v[g], y[:, :, :]).then_inc(y_stored, 16)

            def pair(i, layer, before):
                for par in range(2):
                    g = 2 * i + par
                    first = before is None and par == 0
                    turn = before is not None and before != layer and par == 0
                    for k in range(BATCHES):
                        n = g * BATCHES + k
                        even = g * (BATCHES // 2) + k // 2
                        parts = slice(0, SPLITS - 1 if by_vector(k) else SPLITS)
                        if turn and (k == 0 or k % PER_CHUNK == 1 and k // PER_CHUNK + 1 < PIECES):
                            prepare(PIECES + (k + 1) // PER_CHUNK)
                        if not (first and k < PARTS):
                            act.wait_ge(highs_used, n - PARTS + 1)
                            act.wait_ge(low_ready, n - PARTS + 1)
                            if by_vector(k):
                                act.wait_ge(low_ps_ready, even)
                        act.wait_ge(turned_ready, n + 1)
                        nc.scalar.copy(high[:, k % PARTS, parts, :],
                                       turned[k % TURNED][:, 1:, :]).then_inc(high_ready, 1)
                        if by_vector(k):
                            act.wait_ge(turned_ps_ready, even + 1)
                            nc.scalar.copy(high[:, k % PARTS, SPLITS - 1, :],
                                           turned_ps[k // 2 % 2][:, :]).then_inc(high_ps_ready, 1)
                        if first and k < RING - 2:
                            load_adj(act, (2, 3), 0, 2 + k, 2 + k)
                        if first and k % 2 == 1 and 2 + k // 2 < PIECES:
                            prepare(2 + k // 2)
                        if k % PER_CHUNK == PER_CHUNK - 1:
                            p = k // PER_CHUNK
                            before_turn = isinstance(g, int) and g == BLOCKS - 1
                            final = isinstance(g, int) and g == 2 * BLOCKS - 1
                            if turn and p + HELD < CHUNKS - HELD:
                                load_adj(act, (2, 3), rows_of(g, layer), chunk_at(p + HELD, True),
                                         slot_at(p, True))
                            elif not turn and p + RING < CHUNKS:
                                load_adj(act, (2, 3), rows_of(g, layer), p + RING, p % RING)
                            elif not (before_turn or final):
                                c = p + RING - CHUNKS
                                load_adj(act, (2, 3), rows_of(g + 1, layer), c, c)
                        if par == 1:
                            finish(k, g - 1, layer, 0, i, kept_at(i, par, layer, before))
                        elif before is not None:
                            finish(k, g - 1, before, 1, i, kept_at(i, par, layer, before))

            load_stage(act, x, 1, 1)
            load_adj(act, (2, 3), 0, 0, 0)
            load_adj(act, (2, 3), 0, 1, 1)
            act.wait_ge(eps_ready, 1)
            prepare(0)
            prepare(1)
            walk(act, pair)
            for k in range(BATCHES):
                finish(k, 2 * BLOCKS - 1, 2, 1, 2 * PAIRS, None)

        @block.gpsimd
        def _(pool):
            def prepare(q):
                s = q % 2
                pool.wait_ge(op_high, q + 1)
                splits = slice(q * PER_CHUNK * SPLITS, (q + 1) * PER_CHUNK * SPLITS)
                view = op_split[:, splits, :, :].rearrange("p (k s) h f -> p k s h f", s=SPLITS)
                for k in range(PER_CHUNK):
                    last = nc.gpsimd.tensor_tensor(view[:, k, :, 1, :],
                                                   stage[:, s, k * BATCH + 1:(k + 1) * BATCH, :],
                                                   view[:, k, :, 0, :].bitcast(F32), ALU.subtract)
                last.then_inc(x_low, 1)

            def pair(i, layer, before):
                for par in range(2):
                    g = 2 * i + par
                    first = before is None and par == 0
                    turn = before is not None and before != layer and par == 0
                    for k in range(BATCHES):
                        n = g * BATCHES + k
                        parts = slice(0, SPLITS - 1 if by_vector(k) else SPLITS)
                        pool.wait_ge(high_ready, n + 1)
                        if not (first and k < PARTS):
                            pool.wait_ge(multiplied, n - PARTS + 1)
                        nc.gpsimd.tensor_tensor(low[:, k % PARTS, parts, :], turned[k % TURNED][:, 1:, :],
                                                high[:, k % PARTS, parts, :].bitcast(F32),
                                                ALU.subtract).then_inc(low_ready, 1)
                        if first and k % 2 == 1 and 2 + k // 2 < PIECES:
                            prepare(2 + k // 2)

            nc.gpsimd.memset(ident[:, :], 0.0).then_inc(ident_zero, 1)
            pool.wait_ge(ident_zero, 1)
            nc.gpsimd.affine_select(out=ident[:, :], in_=ident[:, :], compare_op=ALU.not_equal, fill=1.0, base=0,
                                    pattern=[[-1, P]], channel_multiplier=1).then_inc(ident_ready, 1)
            prepare(0)
            prepare(1)
            walk(pool, pair)

        @block.tensor
        def _(pe):
            def finish(k, g, layer):
                if k == 1:
                    pe.wait_ge(acc_copied, g + 1)
                    for t in range(TILES):
                        last = nc.tensor.transpose(nat[:, t, :], acc_rows[:, t, :], ident[:, :])
                    last.then_inc(nat_ready, 1)
                if k == 6 and layer == 1:
                    pe.wait_ge(normed_ready, g + 1)
                    for t in range(TILES):
                        last = nc.tensor.transpose(x1T_ps[:, t * P:(t + 1) * P], normed[:, t, :], ident[:, :])
                    last.then_inc(x1T_ready, 1)
                if k == 7 and layer == 1:
                    pe.wait_ge(x1T_copied, g + 1)
                    for t in range(TILES):
                        last = nc.tensor.matmul(fc_ps[:, t, :], acc_sb[:, t * P:(t + 1) * P], w_sb[:, :],
                                                start=True, stop=True)
                    last.then_inc(fc_done, 1)

            def highs(n, k, kc, even, to):
                pe.wait_ge(turned_ready, n + 1)
                nc.tensor.matmul(to, op_full[:, kc, :], turned[k % TURNED][:, 0, :], start=k == 0, stop=False)
                pe.wait_ge(high_ready, n + 1)
                for s in range(SPLITS):
                    if s == SPLITS - 1 and by_vector(k):
                        pe.wait_ge(high_ps_ready, even + 1)
                    for part in (1, 0):
                        last = nc.tensor.matmul(to, op_split[:, kc * SPLITS + s, part, :], high[:, k % PARTS, s, :],
                                                start=False, stop=False)
                last.then_inc(highs_used, 1)

            def lows(n, k, kc, even, to):
                pe.wait_ge(low_ready, n + 1)
                for s in range(SPLITS):
                    if s == SPLITS - 1 and by_vector(k):
                        pe.wait_ge(low_ps_ready, even + 1)
                    last = nc.tensor.matmul(to, op_split[:, kc * SPLITS + s, 0, :], low[:, k % PARTS, s, :],
                                            start=False, stop=k == BATCHES - 1 and s == SPLITS - 1)
                last.then_inc(multiplied, 1)

            def pair(i, layer, before):
                for par in range(2):
                    g = 2 * i + par
                    first = before is None and par == 0
                    turn = before is not None and before != layer and par == 0
                    for k in range(BATCHES):
                        n = g * BATCHES + k
                        even = g * (BATCHES // 2) + k // 2
                        if first and k % PER_CHUNK == 0:
                            pe.wait_ge(op_full_ready, k // PER_CHUNK + 1)
                            pe.wait_ge(x_low, k // PER_CHUNK + 1)
                        if turn and k % PER_CHUNK == 0:
                            pe.wait_ge(op_full_ready, PIECES + k // PER_CHUNK + 1)
                            pe.wait_ge(y_low, k // PER_CHUNK + 1)
                        highs(n, k, batch_at(k, turn), even, acc[par][:, :])
                        if k > 0:
                            lows(n - 1, k - 1, batch_at(k - 1, turn), even, acc[par][:, :])
                        elif not first:
                            lows(n - 1, BATCHES - 1, BATCHES - 1, even - 1, acc[1 - par][:, :])
                        if par == 1:
                            finish(k, g - 1, layer)
                        elif before is not None:
                            finish(k, g - 1, before)

            pe.wait_ge(ident_ready, 1)
            pe.wait_ge(const_loaded, 32)
            walk(pe, pair)
            lows(2 * BLOCKS * BATCHES - 1, BATCHES - 1, BATCHES - 1, 0, acc[1][:, :])
            for k in range(BATCHES):
                finish(k, 2 * BLOCKS - 1, 2)


_INS = ['x', 'adj', 'L0_gnn_h', 'L1_gnn_W', 'L1_gnn_b']


def kernel(**inputs):
    import numpy as _np
    import concourse.bacc as _bacc
    from concourse import mybir as _mybir
    from concourse.bass_utils import run_bass_kernel_spmd as _run

    nc = _bacc.Bacc("TRN2", target_bir_lowering=False, num_devices=1)
    arrays, args = {}, []
    for name in _INS:
        a = _np.ascontiguousarray(inputs[name])
        arrays[f"in_{name}_dram"] = a
        args.append(nc.dram_tensor(f"in_{name}_dram", a.shape, _mybir.dt.from_np(a.dtype), kind="ExternalInput").ap())
    out = nc.dram_tensor("out_0_dram", inputs["x"].shape, _mybir.dt.float32, kind="ExternalOutput").ap()
    bass_adj_resnorm(nc, *args, out)
    r = _run(nc, [arrays], core_ids=[0])
    return r.results[0]["out_0_dram"]
```
